# Optimizing a Trainium2 kernel written in Bass

```python
import numpy as np
import jax
import jax.numpy as jnp

def _softmax(x, axis=-1):
    return jax.nn.softmax(x, axis=axis)

def _gelu(x):
    return jax.nn.gelu(x, approximate=True)

def _silu(x):
    return jax.nn.silu(x)

def _sigmoid(x):
    return jax.nn.sigmoid(x)

def _layernorm(x, axis=-1, eps=1e-05):
    m = jnp.mean(x, axis=axis, keepdims=True)
    v = jnp.var(x, axis=axis, keepdims=True)
    return (x - m) / jnp.sqrt(v + eps)

def _scatter_add(tgt, idx, src, axis=0):
    return tgt.at[idx].add(src)

def _segment_sum(src, seg, n):
    return jax.ops.segment_sum(src, seg, n)
kernel_name = 'mk_dlrm_tower_d1_rec_r8_a74ac0'

def setup_inputs(seed: int=0):
    np.random.seed(seed)
    _w = jnp.asarray

    def _rec_inputs():
        import jax
        import jax.numpy as jnp
        _tk = jax.random.key(seed)
        ids = jnp.stack([jax.random.randint(jax.random.fold_in(_tk, 200 + f), (512,), 0, v, jnp.int32) for f, v in enumerate([1000, 125000, 12500, 1000, 1250, 12500, 12500, 1000, 1250, 1000, 12500, 12500, 1000, 1250, 1250, 1000, 1000, 12500, 1000, 12500, 1250, 1000, 12500, 1000, 1250, 1250])], axis=1)
        tbl_0 = 0.05 * jax.random.normal(jax.random.fold_in(_tk, 500 + 0), (1000, 128), jnp.float32)
        tbl_1 = 0.05 * jax.random.normal(jax.random.fold_in(_tk, 500 + 1), (125000, 128), jnp.float32)
        tbl_2 = 0.05 * jax.random.normal(jax.random.fold_in(_tk, 500 + 2), (12500, 128), jnp.float32)
        tbl_3 = 0.05 * jax.random.normal(jax.random.fold_in(_tk, 500 + 3), (1000, 128), jnp.float32)
        tbl_4 = 0.05 * jax.random.normal(jax.random.fold_in(_tk, 500 + 4), (1250, 128), jnp.float32)
        tbl_5 = 0.05 * jax.random.normal(jax.random.fold_in(_tk, 500 + 5), (12500, 128), jnp.float32)
        tbl_6 = 0.05 * jax.random.normal(jax.random.fold_in(_tk, 500 + 6), (12500, 128), jnp.float32)
        tbl_7 = 0.05 * jax.random.normal(jax.random.fold_in(_tk, 500 + 7), (1000, 128), jnp.float32)
        tbl_8 = 0.05 * jax.random.normal(jax.random.fold_in(_tk, 500 + 8), (1250, 128), jnp.float32)
        tbl_9 = 0.05 * jax.random.normal(jax.random.fold_in(_tk, 500 + 9), (1000, 128), jnp.float32)
        tbl_10 = 0.05 * jax.random.normal(jax.random.fold_in(_tk, 500 + 10), (12500, 128), jnp.float32)
        tbl_11 = 0.05 * jax.random.normal(jax.random.fold_in(_tk, 500 + 11), (12500, 128), jnp.float32)
        tbl_12 = 0.05 * jax.random.normal(jax.random.fold_in(_tk, 500 + 12), (1000, 128), jnp.float32)
        tbl_13 = 0.05 * jax.random.normal(jax.random.fold_in(_tk, 500 + 13), (1250, 128), jnp.float32)
        tbl_14 = 0.05 * jax.random.normal(jax.random.fold_in(_tk, 500 + 14), (1250, 128), jnp.float32)
        tbl_15 = 0.05 * jax.random.normal(jax.random.fold_in(_tk, 500 + 15), (1000, 128), jnp.float32)
        tbl_16 = 0.05 * jax.random.normal(jax.random.fold_in(_tk, 500 + 16), (1000, 128), jnp.float32)
        tbl_17 = 0.05 * jax.random.normal(jax.random.fold_in(_tk, 500 + 17), (12500, 128), jnp.float32)
        tbl_18 = 0.05 * jax.random.normal(jax.random.fold_in(_tk, 500 + 18), (1000, 128), jnp.float32)
        tbl_19 = 0.05 * jax.random.normal(jax.random.fold_in(_tk, 500 + 19), (12500, 128), jnp.float32)
        tbl_20 = 0.05 * jax.random.normal(jax.random.fold_in(_tk, 500 + 20), (1250, 128), jnp.float32)
        tbl_21 = 0.05 * jax.random.normal(jax.random.fold_in(_tk, 500 + 21), (1000, 128), jnp.float32)
        tbl_22 = 0.05 * jax.random.normal(jax.random.fold_in(_tk, 500 + 22), (12500, 128), jnp.float32)
        tbl_23 = 0.05 * jax.random.normal(jax.random.fold_in(_tk, 500 + 23), (1000, 128), jnp.float32)
        tbl_24 = 0.05 * jax.random.normal(jax.random.fold_in(_tk, 500 + 24), (1250, 128), jnp.float32)
        tbl_25 = 0.05 * jax.random.normal(jax.random.fold_in(_tk, 500 + 25), (1250, 128), jnp.float32)
        _rk = jax.random.fold_in(_tk, 7)
        r_dense_x = -0.000514642 + 1.00011 * jax.random.normal(jax.random.fold_in(_rk, 101), (512, 128), jnp.float32)
        W_top1 = 0.0456912 * jax.random.normal(jax.random.fold_in(_tk, 801), (479, 512), jnp.float32)
        W_top2 = 0.0441942 * jax.random.normal(jax.random.fold_in(_tk, 802), (512, 256), jnp.float32)
        W_top3 = 0.0625 * jax.random.normal(jax.random.fold_in(_tk, 803), (256, 1), jnp.float32)
        b_top1 = jnp.zeros((512,), jnp.float32)
        b_top2 = jnp.zeros((256,), jnp.float32)
        return (r_dense_x, ids, tbl_0, tbl_1, tbl_2, tbl_3, tbl_4, tbl_5, tbl_6, tbl_7, tbl_8, tbl_9, tbl_10, tbl_11, tbl_12, tbl_13, tbl_14, tbl_15, tbl_16, tbl_17, tbl_18, tbl_19, tbl_20, tbl_21, tbl_22, tbl_23, tbl_24, tbl_25, W_top1, b_top1, W_top2, b_top2, W_top3)
    r_dense_x, ids, tbl_0, tbl_1, tbl_2, tbl_3, tbl_4, tbl_5, tbl_6, tbl_7, tbl_8, tbl_9, tbl_10, tbl_11, tbl_12, tbl_13, tbl_14, tbl_15, tbl_16, tbl_17, tbl_18, tbl_19, tbl_20, tbl_21, tbl_22, tbl_23, tbl_24, tbl_25, W_top1, b_top1, W_top2, b_top2, W_top3 = _rec_inputs()

    def _L0_rec_setup():
        import jax, jax.numpy as jnp
        import numpy as np
        F = 26
        D = 128
        B = 2048
        _TRIU_I, _TRIU_J = np.triu_indices(F + 1, k=1)
        _TRIU_I = jnp.asarray(_TRIU_I)
        _TRIU_J = jnp.asarray(_TRIU_J)
        key = jax.random.key(seed)
        k1, k2 = jax.random.split(key)
        sparse_x = jax.random.normal(k1, (B, F, D), dtype=jnp.float32)
        dense_x = jax.random.normal(k2, (B, D), dtype=jnp.float32)
        return {'sparse_x': sparse_x, 'dense_x': dense_x}
    _L0_rec_all = _L0_rec_setup()
    _L0_rec_in = {k: v for k, v in _L0_rec_all.items() if k in ()}
    del _L0_rec_all
    return {'r_dense_x': r_dense_x, 'ids': ids, 'tbl_0': tbl_0, 'tbl_1': tbl_1, 'tbl_2': tbl_2, 'tbl_3': tbl_3, 'tbl_4': tbl_4, 'tbl_5': tbl_5, 'tbl_6': tbl_6, 'tbl_7': tbl_7, 'tbl_8': tbl_8, 'tbl_9': tbl_9, 'tbl_10': tbl_10, 'tbl_11': tbl_11, 'tbl_12': tbl_12, 'tbl_13': tbl_13, 'tbl_14': tbl_14, 'tbl_15': tbl_15, 'tbl_16': tbl_16, 'tbl_17': tbl_17, 'tbl_18': tbl_18, 'tbl_19': tbl_19, 'tbl_20': tbl_20, 'tbl_21': tbl_21, 'tbl_22': tbl_22, 'tbl_23': tbl_23, 'tbl_24': tbl_24, 'tbl_25': tbl_25, 'W_top1': W_top1, 'b_top1': b_top1, 'W_top2': W_top2, 'b_top2': b_top2, 'W_top3': W_top3}

def reference(r_dense_x, ids, tbl_0, tbl_1, tbl_2, tbl_3, tbl_4, tbl_5, tbl_6, tbl_7, tbl_8, tbl_9, tbl_10, tbl_11, tbl_12, tbl_13, tbl_14, tbl_15, tbl_16, tbl_17, tbl_18, tbl_19, tbl_20, tbl_21, tbl_22, tbl_23, tbl_24, tbl_25, W_top1, b_top1, W_top2, b_top2, W_top3):
    import jax
    import jax.numpy as jnp

    def _L0_rec_ref(sparse_x, dense_x):
        import jax, jax.numpy as jnp
        import numpy as np
        F = 26
        D = 128
        B = 2048
        _TRIU_I, _TRIU_J = np.triu_indices(F + 1, k=1)
        _TRIU_I = jnp.asarray(_TRIU_I)
        _TRIU_J = jnp.asarray(_TRIU_J)
        combined = jnp.concatenate([sparse_x, dense_x[:, None, :]], axis=1)
        interact = jnp.einsum('bfd,bgd->bfg', combined, combined)
        return interact[:, _TRIU_I, _TRIU_J]
    e = jnp.stack([tbl_0[ids[:, 0]], tbl_1[ids[:, 1]], tbl_2[ids[:, 2]], tbl_3[ids[:, 3]], tbl_4[ids[:, 4]], tbl_5[ids[:, 5]], tbl_6[ids[:, 6]], tbl_7[ids[:, 7]], tbl_8[ids[:, 8]], tbl_9[ids[:, 9]], tbl_10[ids[:, 10]], tbl_11[ids[:, 11]], tbl_12[ids[:, 12]], tbl_13[ids[:, 13]], tbl_14[ids[:, 14]], tbl_15[ids[:, 15]], tbl_16[ids[:, 16]], tbl_17[ids[:, 17]], tbl_18[ids[:, 18]], tbl_19[ids[:, 19]], tbl_20[ids[:, 20]], tbl_21[ids[:, 21]], tbl_22[ids[:, 22]], tbl_23[ids[:, 23]], tbl_24[ids[:, 24]], tbl_25[ids[:, 25]]], axis=1)
    z = _L0_rec_ref(e, r_dense_x)
    z = z.reshape(z.shape[0], -1)
    h = jnp.concatenate([z, r_dense_x], axis=1)
    h = jnp.maximum(h @ W_top1 + b_top1, 0.0)
    h = jnp.maximum(h @ W_top2 + b_top2, 0.0)
    y = h @ W_top3
    return y

_drawn_inputs = setup_inputs


def setup_inputs(seed=0):
    import zlib

    import numpy as np

    out = dict(_drawn_inputs(seed))
    spreads = {'b_top1': (0.0, 0.1), 'b_top2': (0.0, 0.1)}
    factors = {}
    for name, (base, spread) in spreads.items():
        noise = np.random.default_rng([zlib.crc32(name.encode()), seed]).standard_normal(out[name].shape)
        drawn = base * np.exp(spread * noise) if base else spread * noise
        out[name] = jnp.asarray(drawn.astype(out[name].dtype))
    for name, factor in factors.items():
        out[name] = (out[name] * factor).astype(out[name].dtype)
    return out
```

```python
from contextlib import ExitStack

import concourse.bass as bass
from concourse import mybir

BATCH, DIM, TABLES = 512, 128, 26
P = 128
TILES = BATCH // P
FEATS = TABLES + 1
SUB = 32
GROUPS = P // SUB
DENSE = TABLES
PER_BANK = 4
BLOCKS = -(-FEATS // PER_BANK)
GRAM_BANK = 16
HID1, HID2 = 512, 256
N1, N2 = HID1 // P, HID2 // P
TWOS = TABLES // 2
WIDTH = [2 * a + 2 for a in range(TWOS)]
START = [sum(2 * w for w in WIDTH[:a]) for a in range(TWOS)]
PAIR_CHUNKS = -(-(2 * sum(WIDTH)) // P)
SLOTS = PAIR_CHUNKS * P
K1 = PAIR_CHUNKS + 1
REGROUPS = -(-TWOS // 2)
HALF = 2


def tower(nc, ids, dense, tables, w1, b1, w2, b2, w3, out):
    f32, i32 = mybir.dt.float32, mybir.dt.int32
    ACT, ALU = mybir.ActivationFunctionType, mybir.AluOpType
    ids_of = ids.rearrange("(p t) f -> p t f", t=TILES)
    dense_of = dense.rearrange("(p t) d -> p t d", t=TILES)

    with ExitStack() as ctx:
        def sb(name, shape, dt=f32):
            return ctx.enter_context(nc.sbuf_tensor(name, shape, dt))

        def bank(name, shape):
            return ctx.enter_context(nc.psum_tensor(name, shape, f32))

        def sem(name):
            return ctx.enter_context(nc.semaphore(name))

        ids_now = sb("ids_now", [P, HALF, TABLES], i32)
        emb = sb("emb", [P, HALF, FEATS, DIM])
        feats_t = [sb(f"feats_t{u}", [P, P, SUB]) for u in range(HALF)]
        dense_t = sb("dense_t", [P, HALF, P])
        gram = sb("gram", [P, FEATS, SUB])
        pairs = sb("pairs", [SUB, GROUPS, SLOTS])
        pairs_t = sb("pairs_t", [P, PAIR_CHUNKS, P])
        h1 = sb("h1", [P, N1, P])
        h2 = sb("h2", [P, N2, P])
        y_all = sb("y_all", [P, TILES])
        w1_sb = sb("w1_sb", [P, K1, HID1])
        w2_sb = sb("w2_sb", [P, N1, HID2])
        w3_sb = sb("w3_sb", [P, N2])
        b1_sb = sb("b1_sb", [P, N1])
        b2_sb = sb("b2_sb", [P, N2])
        ident = sb("ident", [P, P])

        block_ps = [bank(f"block_ps{k}", [P, PER_BANK, P]) for k in range(2)]
        gram_ps = [bank(f"gram_ps{k}", [P, GRAM_BANK, FEATS]) for k in range(2)]
        col_ps = bank("col_ps", [P, 4, P])
        back_ps = bank("back_ps", [P, 4, P])
        h1_ps = bank("h1_ps", [P, N1, P])
        h2_ps = bank("h2_ps", [P, N2 + 1, P])
        turn_ps = [col_ps, back_ps]

        ids_loaded = [sem(f"ids_loaded{u}") for u in range(HALF)]
        gathering = sem("gathering")
        rows_in = [[sem(f"rows_in{u}_{q}") for q in range(BLOCKS)] for u in range(HALF)]
        dense_in = [sem(f"dense_in{u}") for u in range(HALF)]
        weights_in = sem("weights_in")
        ident_blank, ident_set = sem("ident_blank"), sem("ident_set")
        pads_set = sem("pads_set")
        blocks_up = sem("blocks_up")
        dve_blocks, act_blocks = sem("dve_blocks"), sem("act_blocks")
        grams_up = sem("grams_up")
        dve_grams, act_grams = sem("dve_grams"), sem("act_grams")
        cols_up = sem("cols_up")
        dve_cols, act_cols = sem("dve_cols"), sem("act_cols")
        regrouping = sem("regrouping")
        back_up, pairs_ready = sem("back_up"), sem("pairs_ready")
        h1_up, h1_ready = sem("h1_up"), sem("h1_ready")
        h2_up, h2_ready = sem("h2_up"), sem("h2_ready")
        y_up, y_ready = sem("y_up"), sem("y_ready")
        stored = sem("stored")

        DB, AB = (BLOCKS + 1) // 2, BLOCKS // 2
        DC, AC = (REGROUPS + 1) // 2, REGROUPS // 2

        def block_feats(q):
            return range(PER_BANK * q, min(PER_BANK * (q + 1), FEATS))

        def spread(q, u):
            n = len(block_feats(q))
            return (feats_t[u][:, :, PER_BANK * q:PER_BANK * q + n],
                    block_ps[q % 2][:, 0:n, :].rearrange("d f p -> d p f"))

        def gram_bank(k):
            return (gram[:, :, GRAM_BANK * k:GRAM_BANK * (k + 1)],
                    gram_ps[k][:, :, :].rearrange("r g j -> r j g"))

        def kept(a):
            w = WIDTH[a]
            return (pairs[:, :, START[a]:START[a] + 2 * w].rearrange("g s (j f) -> g j s f", j=2),
                    turn_ps[(a // 2) % 2][0:SUB, 2 * (a % 2):2 * (a % 2) + 2, :]
                    .rearrange("g j (s f) -> g j s f", s=GROUPS)[:, :, :, 0:w])

        def twos_of(r):
            return range(2 * r, min(2 * r + 2, TWOS))

        block = ctx.enter_context(nc.Block())

        @block.sync
        def _(sp):
            def load_tile(t):
                u = t % HALF
                sp.dma_start(ids_now[:, u, :], ids_of[:, t, :]).then_inc(ids_loaded[u], 16)
                sp.dma_start(emb[:, u, DENSE, :], dense_of[:, t, :]).then_inc(dense_in[u], 16)

            for t in range(HALF):
                load_tile(t)
            sp.dma_start(w1_sb[:, :, :], w1).then_inc(weights_in, 16)
            sp.dma_start(w2_sb[:, :, :], w2).then_inc(weights_in, 16)
            sp.dma_start(w3_sb[:, :], w3).then_inc(weights_in, 16)
            sp.dma_start(b1_sb[:, :], b1).then_inc(weights_in, 16)
            sp.dma_start(b2_sb[:, :], b2).then_inc(weights_in, 16)
            for t in range(HALF, TILES):
                sp.wait_ge(blocks_up, BLOCKS * (t - HALF + 1))
                load_tile(t)
            sp.wait_ge(y_ready, 1 + TILES)
            sp.dma_start(out.rearrange("(p t) n -> p (t n)", t=TILES), y_all[:, :]).then_inc(stored, 16)
            sp.wait_ge(stored, 16)

        @block.gpsimd
        def _(pool):
            pool.wait_ge(ident_blank, 1)
            nc.gpsimd.affine_select(out=ident[:, :], in_=ident[:, :], compare_op=ALU.not_equal, fill=1.0,
                                    base=0, pattern=[[-1, P]], channel_multiplier=1).then_inc(ident_set, 1)
            with pool.Fori(0, TILES // HALF) as i:
                for u in range(HALF):
                    pool.wait_ge(ids_loaded[u], 16 * (i + 1))
                    pool.sem_inc(gathering, 1)
                    for f in range(TABLES):
                        nc.gpsimd.indirect_dma_start(
                            emb[:, u, f, :], None, tables[f],
                            bass.IndirectOffsetOnAxis(ap=ids_now[:, u, f:f + 1], axis=0),
                        ).then_inc(rows_in[u][f // PER_BANK], 16)

        @block.vector
        def _(dve):
            for free in (dve_blocks, dve_cols, pairs_ready, y_ready):
                dve.sem_inc(free, 1)
            nc.vector.memset(ident[:, :], 0.0).then_inc(ident_blank, 1)
            for u in range(HALF):
                nc.vector.memset(feats_t[u][:, :, FEATS:SUB], 0.0).then_inc(pads_set, 1)
            nc.vector.memset(pairs[:, :, 2 * sum(WIDTH):SLOTS], 0.0).then_inc(pads_set, 1)
            with dve.Fori(0, TILES // HALF) as i:
                for u in range(HALF):
                    t = HALF * i + u
                    for q in range(0, BLOCKS, 2):
                        dve.wait_ge(blocks_up, BLOCKS * t + q + 1)
                        dst, src = spread(q, u)
                        last = nc.vector.tensor_copy(dst, src)
                        if DENSE in block_feats(q):
                            last = nc.vector.tensor_copy(dense_t[:, u, :], block_ps[q % 2][:, DENSE % PER_BANK, :])
                        last.then_inc(dve_blocks, 1)
                    dve.wait_ge(grams_up, 2 * t + 1)
                    dst, src = gram_bank(0)
                    nc.vector.tensor_copy(dst, src).then_inc(dve_grams, 1)
                    for r in range(0, REGROUPS, 2):
                        dve.wait_ge(cols_up, REGROUPS * t + r + 1)
                        for a in twos_of(r):
                            dst, src = kept(a)
                            last = nc.vector.tensor_copy(dst, src)
                        last.then_inc(dve_cols, 1)
                    dve.wait_ge(back_up, t + 1)
                    nc.vector.tensor_copy(pairs_t[:, :, :], back_ps[:, 0:PAIR_CHUNKS, :]).then_inc(pairs_ready, 1)
                    dve.wait_ge(h2_up, t + 1)
                    for m in range(N2):
                        last = nc.vector.tensor_scalar(h2[:, m, :], h2_ps[:, m, :], b2_sb[:, m:m + 1], 0.0,
                                                       ALU.add, ALU.max)
                    last.then_inc(h2_ready, 1)
                    dve.wait_ge(y_up, t + 1)
                    nc.vector.tensor_copy(y_all[:, bass.ds(t, 1)], h2_ps[:, N2, 0:1]).then_inc(y_ready, 1)

        @block.scalar
        def _(act):
            for free in (act_blocks, act_cols, h1_ready):
                act.sem_inc(free, 1)
            act.wait_ge(weights_in, 16 * 5)
            with act.Fori(0, TILES // HALF) as i:
                for u in range(HALF):
                    t = HALF * i + u
                    for q in range(1, BLOCKS, 2):
                        act.wait_ge(blocks_up, BLOCKS * t + q + 1)
                        dst, src = spread(q, u)
                        nc.scalar.copy(dst, src).then_inc(act_blocks, 1)
                    act.wait_ge(grams_up, 2 * t + 2)
                    dst, src = gram_bank(1)
                    nc.scalar.copy(dst, src).then_inc(act_grams, 1)
                    for r in range(1, REGROUPS, 2):
                        act.wait_ge(cols_up, REGROUPS * t + r + 1)
                        for a in twos_of(r):
                            dst, src = kept(a)
                            last = nc.scalar.copy(dst, src)
                        last.then_inc(act_cols, 1)
                    act.wait_ge(h1_up, t + 1)
                    for n in range(N1):
                        last = nc.scalar.activation(h1[:, n, :], h1_ps[:, n, :], ACT.Relu, bias=b1_sb[:, n:n + 1])
                    last.then_inc(h1_ready, 1)

        @block.tensor
        def _(pe):
            pe.wait_ge(ident_set, 1)
            pe.wait_ge(pads_set, HALF + 1)
            pe.wait_ge(weights_in, 16 * 5)
            with pe.Fori(0, TILES // HALF) as i:
                for u in range(HALF):
                    t = HALF * i + u
                    for q in range(BLOCKS):
                        gathers = sum(f < TABLES for f in block_feats(q))
                        pe.wait_ge(rows_in[u][q], 16 * gathers * (i + 1))
                        if DENSE in block_feats(q):
                            pe.wait_ge(dense_in[u], 16 * (i + 1))
                        if q % 2 == 0:
                            pe.wait_ge(dve_blocks, 1 + DB * t + q // 2)
                        else:
                            pe.wait_ge(act_blocks, 1 + AB * t + q // 2)
                        for f in block_feats(q):
                            last = nc.tensor.transpose(block_ps[q % 2][:, f % PER_BANK, :], emb[:, u, f, :],
                                                       ident[:, :])
                        last.then_inc(blocks_up, 1)
                    pe.wait_ge(dve_blocks, 1 + DB * (t + 1))
                    pe.wait_ge(act_blocks, 1 + AB * (t + 1))
                    for k in range(2):
                        for g in range(GRAM_BANK):
                            for s in range(GROUPS):
                                p = SUB * s + GRAM_BANK * k + g
                                last = nc.tensor.matmul(gram_ps[k][SUB * s:SUB * (s + 1), g, :],
                                                        feats_t[u][:, p, :], feats_t[u][:, p, 0:FEATS],
                                                        start=True, stop=True)
                        last.then_inc(grams_up, 1)
                    pe.wait_ge(dve_grams, t + 1)
                    pe.wait_ge(act_grams, t + 1)
                    for r in range(REGROUPS):
                        if r % 2 == 0:
                            pe.wait_ge(dve_cols, 1 + DC * t + r // 2)
                        else:
                            pe.wait_ge(act_cols, 1 + AC * t + r // 2)
                        if r == 1:
                            pe.wait_ge(pairs_ready, t + 1)
                        for a in twos_of(r):
                            for j in range(2):
                                last = nc.tensor.transpose(turn_ps[r % 2][0:SUB, 2 * (a % 2) + j, :],
                                                           gram[:, 2 * a + 1 + j, :], ident[:, :])
                        last.then_inc(cols_up, 1)
                    pe.wait_ge(dve_cols, 1 + DC * (t + 1))
                    pe.wait_ge(act_cols, 1 + AC * (t + 1))
                    pe.sem_inc(regrouping, 1)
                    for c in range(PAIR_CHUNKS):
                        for s in range(GROUPS):
                            last = nc.tensor.transpose(back_ps[:, c, SUB * s:SUB * (s + 1)],
                                                       pairs[:, s, P * c:P * (c + 1)], ident[0:SUB, 0:SUB])
                    last.then_inc(back_up, 1)
                    pe.wait_ge(pairs_ready, t + 2)
                    pe.wait_ge(h1_ready, t + 1)
                    for n in range(N1):
                        for c in range(K1):
                            z = dense_t[:, u, :] if c == PAIR_CHUNKS else pairs_t[:, c, :]
                            last = nc.tensor.matmul(h1_ps[:, n, :], w1_sb[:, c, P * n:P * (n + 1)], z,
                                                    start=(c == 0), stop=(c == K1 - 1))
                    last.then_inc(h1_up, 1)
                    pe.wait_ge(h1_ready, t + 2)
                    pe.wait_ge(y_ready, t + 1)
                    for m in range(N2):
                        for n in range(N1):
                            last = nc.tensor.matmul(h2_ps[:, m, :], w2_sb[:, n, P * m:P * (m + 1)], h1[:, n, :],
                                                    start=(n == 0), stop=(n == N1 - 1))
                    last.then_inc(h2_up, 1)
                    pe.wait_ge(h2_ready, t + 1)
                    for m in range(N2):
                        last = nc.tensor.matmul(h2_ps[:, N2, 0:1], h2[:, m, :], w3_sb[:, m:m + 1],
                                                start=(m == 0), stop=(m == N2 - 1))
                    last.then_inc(y_up, 1)


def kernel(**inputs):
    import numpy as np
    import concourse.bacc as bacc
    from concourse.bass_utils import run_bass_kernel_spmd

    at = {}
    for i in range(FEATS):
        for j in range(i + 1, FEATS):
            at[i, j] = len(at)
    w_top1 = np.asarray(inputs["W_top1"])
    w1 = np.zeros((K1 * P, HID1), w_top1.dtype)
    for a in range(TWOS):
        for j in range(2):
            col = 2 * a + 1 + j
            for i in range(col):
                w1[START[a] + j * WIDTH[a] + i] = w_top1[at[i, col]]
    w1[SLOTS:] = w_top1[len(at):]

    def chunks(a, n):
        return np.ascontiguousarray(np.asarray(a).reshape(n, P, -1).transpose(1, 0, 2))

    arrays = {
        "ids": np.ascontiguousarray(inputs["ids"]),
        "dense": np.ascontiguousarray(inputs["r_dense_x"]),
        "w1": chunks(w1, K1),
        "b1": chunks(inputs["b_top1"], N1).reshape(P, N1),
        "w2": chunks(inputs["W_top2"], N1),
        "b2": chunks(inputs["b_top2"], N2).reshape(P, N2),
        "w3": chunks(inputs["W_top3"], N2).reshape(P, N2),
    }
    for f in range(TABLES):
        arrays[f"tbl_{f}"] = np.ascontiguousarray(inputs[f"tbl_{f}"])

    nc = bacc.Bacc("TRN2", target_bir_lowering=False, num_devices=1)
    ap = {name: nc.dram_tensor(name, a.shape, mybir.dt.from_np(a.dtype), kind="ExternalInput").ap()
          for name, a in arrays.items()}
    out = nc.dram_tensor("out", (BATCH, 1), mybir.dt.float32, kind="ExternalOutput").ap()
    tower(nc, ap["ids"], ap["dense"], [ap[f"tbl_{f}"] for f in range(TABLES)],
          ap["w1"], ap["b1"], ap["w2"], ap["b2"], ap["w3"], out)
    return run_bass_kernel_spmd(nc, [arrays], core_ids=[0]).results[0]["out"]
```

```python
from contextlib import ExitStack

import concourse.bass as bass
from concourse import mybir

BATCH, DIM, TABLES = 512, 128, 26
P = 128
TILES = BATCH // P
FEATS = TABLES + 1
SUB = 32
GROUP = P // SUB
ROWS = (1000, 125000, 12500, 1000, 1250, 12500, 12500, 1000, 1250, 1000, 12500, 12500, 1000,
        1250, 1250, 1000, 1000, 12500, 1000, 12500, 1250, 1000, 12500, 1000, 1250, 1250)
HOT_ROWS = min(ROWS)
LOOKS = 8
HOT_P = HOT_ROWS // LOOKS
HOT = 8
HOT_TABLES = [f for f in range(TABLES) if ROWS[f] == HOT_ROWS][:HOT]
COLD_TABLES = [f for f in range(TABLES) if f not in HOT_TABLES]
COLD = len(COLD_TABLES)
ORDER = HOT_TABLES + COLD_TABLES + [TABLES]
BLOCK = 4
BLOCKS = -(-(COLD + 1) // BLOCK)
ROUND = 8
ROUNDS = SUB // ROUND
REACH = TABLES // 2
WIDE = FEATS + REACH
CHUNK_F = 9
PAIR_CHUNKS = FEATS // CHUNK_F
CHUNK = CHUNK_F * REACH
K1 = PAIR_CHUNKS + 1
HID1, HID2 = 512, 256
N1, N2 = HID1 // P, HID2 // P
BUFS = 2
ACT_LOOKS = 2
DVE_LOOKS = LOOKS - ACT_LOOKS


def tower(nc, ids, hot_ids, dense, hot_tables, tables, w1, b1, w2, b2, w3, out):
    f32, f32r, i32 = mybir.dt.float32, mybir.dt.float32r, mybir.dt.int32
    ACT, ALU = mybir.ActivationFunctionType, mybir.AluOpType

    with ExitStack() as ctx:
        def sb(name, shape, dt=f32):
            return ctx.enter_context(nc.sbuf_tensor(name, shape, dt))

        def ps(name, shape):
            return ctx.enter_context(nc.psum_tensor(name, shape, f32))

        def sem(name):
            return ctx.enter_context(nc.semaphore(name))

        row_of = sb("row_of", [HOT_P, LOOKS])
        hot_ids_now = [sb(f"hot_ids_now{v}", [HOT_P, BATCH], i32) for v in range(BUFS)]
        distance = [sb(f"distance{v}", [HOT_P, ACT_LOOKS, BATCH]) for v in range(BUFS)]
        table = [sb(f"table{v}", [HOT_P, LOOKS, DIM]) for v in range(BUFS)]
        table_hi = [sb(f"table_hi{v}", [HOT_P, LOOKS, DIM], f32r) for v in range(BUFS)]
        table_lo = [sb(f"table_lo{v}", [HOT_P, LOOKS, DIM], f32r) for v in range(BUFS)]
        onehot = [sb(f"onehot{v}", [HOT_P, LOOKS, BATCH], f32r) for v in range(BUFS)]
        ids_all = sb("ids_all", [P, TILES, COLD], i32)
        emb = sb("emb", [P, TILES, COLD + 1, DIM])
        feats_t = sb("feats_t", [P, TILES, SUB, GROUP, SUB])
        dense_t = sb("dense_t", [P, 2, P])
        gram = sb("gram", [P, FEATS, SUB])
        turned = sb("turned", [P, WIDE, SUB])
        pairs = sb("pairs", [P, FEATS, REACH])
        pairs_t = sb("pairs_t", [P, PAIR_CHUNKS, P])
        h1 = sb("h1", [P, N1, P])
        h2 = sb("h2", [P, N2, P])
        y_all = sb("y_all", [P, TILES])
        w1_sb = sb("w1_sb", [P, K1, HID1])
        w2_sb = sb("w2_sb", [P, N1, HID2])
        w3_sb = sb("w3_sb", [P, N2])
        b1_sb = sb("b1_sb", [P, N1])
        b2_sb = sb("b2_sb", [P, N2])
        ident = sb("ident", [P, P])

        block_ps = [ps(f"block_ps{k}", [P, BLOCK, P]) for k in range(2)]
        gram_ps = [ps(f"gram_ps{k}", [P, ROUND, P]) for k in range(2)]
        back_ps = ps("back_ps", [P, PAIR_CHUNKS, P])
        mlp_ps = ps("mlp_ps", [P, N1, P])
        look_ps = [gram_ps[0][:, 4 * v:4 * v + 4, :].rearrange("d t p -> d (t p)") for v in range(BUFS)]

        row_of_set = sem("row_of_set")
        table_in = [sem(f"table_in{v}") for v in range(BUFS)]
        measured = sem("measured")
        hi_ready, lo_ready = sem("hi_ready"), sem("lo_ready")
        dve_onehots, act_onehots = sem("dve_onehots"), sem("act_onehots")
        looked_up = sem("looked_up")
        emptying, looked_ready = sem("emptying"), sem("looked_ready")
        ids_in, dense_in = sem("ids_in"), sem("dense_in")
        rows_in = [[sem(f"rows_in{t}_{q}") for q in range(BLOCKS)] for t in range(TILES)]
        weights_in, biases_in = sem("weights_in"), sem("biases_in")
        ident_blank, ident_set, pads_set = sem("ident_blank"), sem("ident_set"), sem("pads_set")
        blocks_up = sem("blocks_up")
        dve_blocks, act_blocks = sem("dve_blocks"), sem("act_blocks")
        rounds_up = sem("rounds_up")
        dve_rounds, act_rounds = sem("dve_rounds"), sem("act_rounds")
        turned_ready, packed = sem("turned_ready"), sem("packed")
        back_up, pairs_ready = sem("back_up"), sem("pairs_ready")
        h1_up, h1_ready = sem("h1_up"), sem("h1_ready")
        h2_up, h2_ready = sem("h2_up"), sem("h2_ready")
        y_up, y_ready = sem("y_up"), sem("y_ready")
        stored = sem("stored")

        DB, AB = (BLOCKS + 1) // 2, BLOCKS // 2
        DVE_DIAGONAL, ACT_DIAGONAL = range(GROUP // 2), range(GROUP // 2, GROUP)

        def places(q):
            return range(BLOCK * q, min(BLOCK * (q + 1), COLD + 1))

        def spread(q, t):
            n = len(places(q))
            return (feats_t[:, t, :, :, HOT + BLOCK * q:HOT + BLOCK * q + n].rearrange("d g s f -> d s g f"),
                    block_ps[q % 2][:, 0:n, :].rearrange("d f (s g) -> d s g f", g=SUB))

        def diagonal(r, s):
            rows = slice(SUB * s, SUB * (s + 1))
            return (gram[rows, :, ROUND * r:ROUND * (r + 1)].rearrange("f j g -> f g j"),
                    gram_ps[r % 2][rows, :, FEATS * s:FEATS * (s + 1)])

        def all_pairs():
            whole = turned[:, :, :]
            return bass.AP(whole.tensor, whole.offset + SUB, [list(whole.ap[0]), [SUB + 1, FEATS], [SUB, REACH]])

        block = ctx.enter_context(nc.Block())

        @block.sync
        def _(sp):
            def load_table(j):
                v = j % BUFS
                sp.dma_start(table[v][:, :, :], hot_tables[j]).then_inc(table_in[v], 16)
                sp.dma_start(hot_ids_now[v][:, :], hot_ids[j:j + 1, :].to_broadcast((HOT_P, BATCH))
                             ).then_inc(table_in[v], 16)

            sp.dma_start(ids_all[:, :, :], ids).then_inc(ids_in, 16)
            for j in range(BUFS):
                load_table(j)
            sp.dma_start(emb[:, :, COLD, :], dense).then_inc(dense_in, 16)
            for dst, src in ((b1_sb, b1), (b2_sb, b2)):
                sp.dma_start(dst[:], src).then_inc(biases_in, 16)
            for dst, src in ((w1_sb, w1), (w2_sb, w2), (w3_sb, w3)):
                sp.dma_start(dst[:], src).then_inc(weights_in, 16)
            for j in range(BUFS, HOT):
                sp.wait_ge(lo_ready, j - BUFS + 1)
                sp.wait_ge(act_onehots, j - BUFS + 1)
                load_table(j)
            sp.wait_ge(y_ready, TILES)
            sp.dma_start(out.rearrange("(p t) n -> p (t n)", t=TILES), y_all[:, :]).then_inc(stored, 16)
            sp.wait_ge(stored, 16)

        @block.gpsimd
        def _(pool):
            nc.gpsimd.iota(row_of[:, :], [[1, LOOKS]], base=0, channel_multiplier=LOOKS,
                           allow_small_or_imprecise_dtypes=True).then_inc(row_of_set, 1)
            pool.wait_ge(ident_blank, 1)
            nc.gpsimd.affine_select(out=ident[:, :], in_=ident[:, :], compare_op=ALU.not_equal, fill=1.0,
                                    base=0, pattern=[[-1, P]], channel_multiplier=1).then_inc(ident_set, 1)
            pool.wait_ge(ids_in, 16)
            for t in range(TILES):
                for n in range(COLD):
                    nc.gpsimd.indirect_dma_start(
                        emb[:, t, n, :], None, tables[n],
                        bass.IndirectOffsetOnAxis(ap=ids_all[:, t, n:n + 1], axis=0),
                    ).then_inc(rows_in[t][n // BLOCK], 16)

        @block.vector
        def _(dve):
            nc.vector.memset(ident[:, :], 0.0).then_inc(ident_blank, 1)
            nc.vector.memset(feats_t[:, :, :, :, FEATS:SUB], 0.0).then_inc(pads_set, 1)
            dve.wait_ge(row_of_set, 1)
            with dve.Fori(0, HOT // BUFS) as i:
                for v in range(BUFS):
                    j = BUFS * i + v
                    dve.wait_ge(table_in[v], 32 * (i + 1))
                    dve.wait_ge(looked_up, j + 1)
                    for c in range(DVE_LOOKS):
                        nc.vector.tensor_scalar(onehot[v][:, c, :], hot_ids_now[v][:, :],
                                                row_of[:, c:c + 1], None, ALU.is_equal).then_inc(dve_onehots, 1)
                    dve.wait_ge(hi_ready, j + 1)
                    nc.vector.tensor_tensor(table_lo[v][:, :, :], table[v][:, :, :],
                                            table_hi[v][:, :, :].bitcast(f32), ALU.subtract).then_inc(lo_ready, 1)

            def blocks(t, qs):
                for q in qs:
                    dve.wait_ge(blocks_up, BLOCKS * t + q + 1)
                    dst, src = spread(q, t)
                    last = nc.vector.tensor_copy(dst, src)
                    if COLD in places(q):
                        last = nc.vector.tensor_copy(dense_t[:, t % 2, :], block_ps[q % 2][:, COLD % BLOCK, :])
                    last.then_inc(dve_blocks, 1)

            def gram_round(t, r):
                dve.wait_ge(rounds_up, ROUNDS * t + r + 1)
                for s in DVE_DIAGONAL:
                    dst, src = diagonal(r, s)
                    last = nc.vector.tensor_copy(dst, src)
                last.then_inc(dve_rounds, 1)

            def turn(t):
                dve.wait_ge(act_rounds, ROUNDS * (t + 1))
                dve.wait_ge(dve_rounds, ROUNDS * (t + 1))
                nc.vector.transpose(turned[:, 1:FEATS, :], gram[:, 1:FEATS, :])
                nc.vector.transpose(turned[:, FEATS:WIDE, :], gram[:, 0:REACH, :]).then_inc(turned_ready, 1)

            def layer2(t):
                dve.wait_ge(h2_up, t + 1)
                for m in range(N2):
                    last = nc.vector.tensor_scalar(h2[:, m, :], mlp_ps[:, m, :], b2_sb[:, m:m + 1], 0.0,
                                                   ALU.add, ALU.max)
                last.then_inc(h2_ready, 1)

            def layer3(t):
                dve.wait_ge(y_up, t + 1)
                nc.vector.tensor_copy(y_all[:, t:t + 1], mlp_ps[:, N2, 0:1]).then_inc(y_ready, 1)

            dve.wait_ge(biases_in, 16 * 2)
            blocks(0, range(0, BLOCKS, 2))
            for t in range(TILES):
                for r in range(ROUNDS):
                    gram_round(t, r)
                if t + 1 < TILES:
                    blocks(t + 1, [0])
                turn(t)
                if t > 0:
                    layer2(t - 1)
                if t + 1 < TILES:
                    blocks(t + 1, [2])
                if t > 0:
                    layer3(t - 1)
                if t + 1 < TILES:
                    blocks(t + 1, range(4, BLOCKS, 2))
            layer2(TILES - 1)
            layer3(TILES - 1)

        @block.scalar
        def _(act):
            act.sem_inc(looked_ready, BUFS)

            def prepare(v, n):
                j = BUFS * n + v
                act.wait_ge(table_in[v], 32 * (n + 1))
                nc.scalar.copy(table_hi[v][:, :, :], table[v][:, :, :]).then_inc(hi_ready, 1)
                for k in range(ACT_LOOKS):
                    c = DVE_LOOKS + k
                    last = nc.scalar.activation(distance[v][:, k, :], hot_ids_now[v][:, :], ACT.Abs,
                                                bias=row_of[:, c:c + 1], scale=-1.0)
                last.then_inc(measured, 1)
                act.wait_ge(measured, j + 1)
                nc.scalar.activation(onehot[v][:, DVE_LOOKS:LOOKS, :], distance[v][:, :, :], ACT.Relu,
                                     bias=1.0, scale=-1.0).then_inc(act_onehots, 1)

            def empty(v, n):
                j = BUFS * n + v
                act.wait_ge(looked_up, BUFS + j + 1)
                act.sem_inc(emptying, 1)
                dst = feats_t[:, :, :, :, bass.ds(j, 1)].rearrange("d t g s f -> d (t f) s g")
                nc.scalar.copy(dst, look_ps[v].rearrange("d (t s g) -> d t s g", t=TILES, s=GROUP)
                               ).then_inc(looked_ready, 1)

            act.wait_ge(row_of_set, 1)
            prepare(0, 0)
            with act.Fori(0, HOT // BUFS - 1) as i:
                prepare(1, i)
                empty(0, i)
                prepare(0, i + 1)
                empty(1, i)
            prepare(1, HOT // BUFS - 1)
            empty(0, HOT // BUFS - 1)
            empty(1, HOT // BUFS - 1)

            def blocks(t, qs):
                for q in qs:
                    act.wait_ge(blocks_up, BLOCKS * t + q + 1)
                    dst, src = spread(q, t)
                    nc.scalar.copy(dst, src).then_inc(act_blocks, 1)

            def gram_round(t, r):
                act.wait_ge(rounds_up, ROUNDS * t + r + 1)
                if r == 0 and t > 0:
                    act.wait_ge(turned_ready, t)
                for s in ACT_DIAGONAL:
                    dst, src = diagonal(r, s)
                    last = nc.scalar.copy(dst, src)
                last.then_inc(act_rounds, 1)

            def pack(t):
                act.wait_ge(turned_ready, t + 1)
                nc.scalar.copy(pairs[:, :, :], all_pairs()).then_inc(packed, 1)

            def back(t):
                act.wait_ge(back_up, t + 1)
                nc.scalar.copy(pairs_t[0:CHUNK, :, :], back_ps[0:CHUNK, :, :]).then_inc(pairs_ready, 1)

            def layer1(t):
                act.wait_ge(h1_up, t + 1)
                for n in range(N1):
                    last = nc.scalar.activation(h1[:, n, :], mlp_ps[:, n, :], ACT.Relu, bias=b1_sb[:, n:n + 1])
                last.then_inc(h1_ready, 1)

            act.wait_ge(biases_in, 16 * 2)
            blocks(0, range(1, BLOCKS, 2))
            for t in range(TILES):
                gram_round(t, 0)
                if t > 0:
                    layer1(t - 1)
                for r in range(1, ROUNDS):
                    gram_round(t, r)
                if t + 1 < TILES:
                    blocks(t + 1, [1])
                pack(t)
                back(t)
                if t + 1 < TILES:
                    blocks(t + 1, range(3, BLOCKS, 2))
            layer1(TILES - 1)

        @block.tensor
        def _(pe):
            pe.sem_inc(looked_up, BUFS)
            with pe.Fori(0, HOT // BUFS) as i:
                for v in range(BUFS):
                    j = BUFS * i + v
                    pe.wait_ge(looked_ready, j + 1)
                    pe.wait_ge(hi_ready, j + 1)
                    for c in range(LOOKS):
                        if c < DVE_LOOKS:
                            pe.wait_ge(dve_onehots, DVE_LOOKS * j + c + 1)
                        elif c == DVE_LOOKS:
                            pe.wait_ge(act_onehots, j + 1)
                        nc.tensor.matmul(look_ps[v], table_hi[v][:, c, :], onehot[v][:, c, :],
                                         start=(c == 0), stop=False)
                    pe.wait_ge(lo_ready, j + 1)
                    for c in range(LOOKS):
                        last = nc.tensor.matmul(look_ps[v], table_lo[v][:, c, :], onehot[v][:, c, :],
                                                start=False, stop=(c == LOOKS - 1))
                    last.then_inc(looked_up, 1)

            def blocks(t, qs):
                for q in qs:
                    pe.wait_ge(rows_in[t][q], 16 * sum(n < COLD for n in places(q)))
                    if q % 2 == 0 and DB * t + q // 2 > 0:
                        pe.wait_ge(dve_blocks, DB * t + q // 2)
                    if q % 2 == 1 and AB * t + q // 2 > 0:
                        pe.wait_ge(act_blocks, AB * t + q // 2)
                    for n in places(q):
                        last = nc.tensor.transpose(block_ps[q % 2][:, n % BLOCK, :], emb[:, t, n, :], ident[:, :])
                    last.then_inc(blocks_up, 1)

            def gram_rounds(t):
                pe.wait_ge(dve_blocks, DB * (t + 1))
                pe.wait_ge(act_blocks, AB * (t + 1))
                for r in range(ROUNDS):
                    before = ROUNDS * t + r - 2
                    if t == 0 and r == 0:
                        pe.wait_ge(looked_ready, BUFS + HOT)
                    elif before >= 0:
                        pe.wait_ge(dve_rounds, before + 1)
                        pe.wait_ge(act_rounds, before + 1)
                    for k in range(ROUND):
                        g = ROUND * r + k
                        last = nc.tensor.matmul(gram_ps[r % 2][:, k, 0:GROUP * FEATS], feats_t[:, t, g, :, :],
                                                feats_t[:, t, g, :, 0:FEATS], start=True, stop=True)
                    last.then_inc(rounds_up, 1)

            def back(t):
                if t > 0:
                    pe.wait_ge(pairs_ready, t)
                pe.wait_ge(packed, t + 1)
                for c in range(PAIR_CHUNKS):
                    last = nc.tensor.transpose(back_ps[0:CHUNK, c, :], pairs[:, CHUNK_F * c:CHUNK_F * (c + 1), :],
                                               ident[:, :])
                last.then_inc(back_up, 1)

            def layer1_dense(t):
                if t > 0:
                    pe.wait_ge(y_ready, t)
                for n in range(N1):
                    nc.tensor.matmul(mlp_ps[:, n, :], w1_sb[:, PAIR_CHUNKS, P * n:P * (n + 1)], dense_t[:, t % 2, :],
                                     start=(n == 0), stop=False, skip_group_check=True)

            def layer1_pairs(t):
                pe.wait_ge(pairs_ready, t + 1)
                for n in range(N1):
                    for c in range(PAIR_CHUNKS):
                        last = nc.tensor.matmul(mlp_ps[:, n, :], w1_sb[0:CHUNK, c, P * n:P * (n + 1)],
                                                pairs_t[0:CHUNK, c, :], start=False, stop=(c == PAIR_CHUNKS - 1),
                                                skip_group_check=True)
                last.then_inc(h1_up, 1)

            def layer2(t):
                pe.wait_ge(h1_ready, t + 1)
                for m in range(N2):
                    for n in range(N1):
                        last = nc.tensor.matmul(mlp_ps[:, m, :], w2_sb[:, n, P * m:P * (m + 1)], h1[:, n, :],
                                                start=(n == 0), stop=(n == N1 - 1))
                last.then_inc(h2_up, 1)

            def layer3(t):
                pe.wait_ge(h2_ready, t + 1)
                for m in range(N2):
                    last = nc.tensor.matmul(mlp_ps[:, N2, 0:1], h2[:, m, :], w3_sb[:, m:m + 1],
                                            start=(m == 0), stop=(m == N2 - 1))
                last.then_inc(y_up, 1)

            pe.wait_ge(ident_set, 1)
            pe.wait_ge(pads_set, 1)
            pe.wait_ge(dense_in, 16)
            pe.wait_ge(weights_in, 16 * 3)
            blocks(0, range(BLOCKS))
            for t in range(TILES):
                gram_rounds(t)
                if t + 1 < TILES:
                    blocks(t + 1, [0, 1])
                if t > 0:
                    layer2(t - 1)
                if t + 1 < TILES:
                    blocks(t + 1, [2])
                if t > 0:
                    layer3(t - 1)
                layer1_dense(t)
                back(t)
                if t + 1 < TILES:
                    blocks(t + 1, range(3, BLOCKS))
                layer1_pairs(t)
            layer2(TILES - 1)
            layer3(TILES - 1)


def kernel(**inputs):
    import numpy as np
    import concourse.bacc as bacc
    from concourse.bass_utils import run_bass_kernel_spmd

    at = {}
    for i in range(FEATS):
        for j in range(i + 1, FEATS):
            at[i, j] = len(at)
    w_top1 = np.asarray(inputs["W_top1"])
    w1 = np.zeros((K1, P, HID1), w_top1.dtype)
    for f in range(FEATS):
        for delta in range(1, REACH + 1):
            i, j = sorted((ORDER[f], ORDER[(f + delta) % FEATS]))
            w1[f // CHUNK_F, (f % CHUNK_F) * REACH + delta - 1] = w_top1[at[i, j]]
    w1[PAIR_CHUNKS] = w_top1[len(at):]

    def chunks(a, n):
        return np.ascontiguousarray(np.asarray(a).reshape(n, P, -1).transpose(1, 0, 2))

    ids = np.asarray(inputs["ids"]).reshape(P, TILES, TABLES)
    arrays = {
        "ids": np.ascontiguousarray(ids[:, :, COLD_TABLES]),
        "hot_ids": np.ascontiguousarray(ids[:, :, HOT_TABLES].transpose(2, 1, 0)).reshape(HOT, BATCH),
        "dense": np.ascontiguousarray(inputs["r_dense_x"]).reshape(P, TILES, DIM),
        "w1": np.ascontiguousarray(w1.transpose(1, 0, 2)),
        "b1": chunks(inputs["b_top1"], N1).reshape(P, N1),
        "w2": chunks(inputs["W_top2"], N1),
        "b2": chunks(inputs["b_top2"], N2).reshape(P, N2),
        "w3": chunks(inputs["W_top3"], N2).reshape(P, N2),
    }
    for f in range(TABLES):
        shape = (HOT_P, LOOKS, DIM) if f in HOT_TABLES else (ROWS[f], DIM)
        arrays[f"tbl_{f}"] = np.ascontiguousarray(inputs[f"tbl_{f}"]).reshape(shape)

    nc = bacc.Bacc("TRN2", target_bir_lowering=False, num_devices=1)
    ap = {name: nc.dram_tensor(name, a.shape, mybir.dt.from_np(a.dtype), kind="ExternalInput").ap()
          for name, a in arrays.items()}
    out = nc.dram_tensor("out", (BATCH, 1), mybir.dt.float32, kind="ExternalOutput").ap()
    tower(nc, ap["ids"], ap["hot_ids"], ap["dense"], [ap[f"tbl_{f}"] for f in HOT_TABLES],
          [ap[f"tbl_{f}"] for f in COLD_TABLES], ap["w1"], ap["b1"], ap["w2"], ap["b2"], ap["w3"], out)
    return run_bass_kernel_spmd(nc, [arrays], core_ids=[0]).results[0]["out"]
```

```python
from contextlib import ExitStack

import concourse.bass as bass
from concourse import mybir

BATCH, DIM, TABLES = 512, 128, 26
P = 128
TILES = BATCH // P
FEATS = TABLES + 1
SUB = 32
GROUP = P // SUB
ROWS = (1000, 125000, 12500, 1000, 1250, 12500, 12500, 1000, 1250, 1000, 12500, 12500, 1000,
        1250, 1250, 1000, 1000, 12500, 1000, 12500, 1250, 1000, 12500, 1000, 1250, 1250)
HOT_ROWS = min(ROWS)
LOOKS = 8
HOT_P = HOT_ROWS // LOOKS
HOT = 8
HOT_TABLES = [f for f in range(TABLES) if ROWS[f] == HOT_ROWS][:HOT]
COLD_TABLES = [f for f in range(TABLES) if f not in HOT_TABLES]
COLD = len(COLD_TABLES)
ORDER = HOT_TABLES + COLD_TABLES + [TABLES]
BLOCK = 4
BLOCKS = -(-(COLD + 1) // BLOCK)
GRAM_ROWS = SUB * (GROUP - 1) + FEATS
ROUND = 8
ROUNDS = SUB // ROUND
REACH = TABLES // 2
WIDE = FEATS + REACH
CHUNK_F = 9
PAIR_CHUNKS = FEATS // CHUNK_F
CHUNK = CHUNK_F * REACH
TURN = CHUNK_F + REACH
K1 = PAIR_CHUNKS + 1
HID1, HID2 = 512, 256
N1, N2 = HID1 // P, HID2 // P
BUFS = 2
ACT_LOOKS = 2
DVE_LOOKS = LOOKS - ACT_LOOKS
HALF = LOOKS // 2
WARM = 30


def tower(nc, ids, hot_ids, dense, hot_tables, tables, w1, b1, w2, b2, w3, out):
    f32, f32r, i32 = mybir.dt.float32, mybir.dt.float32r, mybir.dt.int32
    ACT, ALU = mybir.ActivationFunctionType, mybir.AluOpType

    with ExitStack() as ctx:
        def sb(name, shape, dt=f32):
            return ctx.enter_context(nc.sbuf_tensor(name, shape, dt))

        def ps(name, shape):
            return ctx.enter_context(nc.psum_tensor(name, shape, f32))

        def sem(name):
            return ctx.enter_context(nc.semaphore(name))

        row_of = sb("row_of", [HOT_P, LOOKS])
        hot_ids_all = sb("hot_ids_all", [HOT_P, HOT, BATCH], i32)
        table = [sb(f"table{v}", [HOT_P, LOOKS, DIM]) for v in range(BUFS)]
        table_hi = [sb(f"table_hi{v}", [HOT_P, LOOKS, DIM], f32r) for v in range(BUFS)]
        table_lo = [sb(f"table_lo{v}", [HOT_P, LOOKS, DIM], f32r) for v in range(BUFS)]
        onehot = [sb(f"onehot{v}", [HOT_P, LOOKS, BATCH], f32r) for v in range(BUFS)]
        ids_all = sb("ids_all", [P, TILES, COLD], i32)
        emb = sb("emb", [P, TILES, COLD + 1, DIM])
        feats_t = sb("feats_t", [P, TILES, SUB, GROUP, SUB])
        dense_t = sb("dense_t", [P, 2, P])
        gram = sb("gram", [P, FEATS, SUB])
        turned = sb("turned", [P, WIDE, SUB])
        pairs = sb("pairs", [P, FEATS, REACH])
        pairs_t = sb("pairs_t", [P, PAIR_CHUNKS, P])
        h1 = sb("h1", [P, N1, P])
        h2 = sb("h2", [P, N2, P])
        y_all = sb("y_all", [P, TILES])
        w1_sb = sb("w1_sb", [P, K1, HID1])
        w2_sb = sb("w2_sb", [P, N1, HID2])
        w3_sb = sb("w3_sb", [P, N2])
        b1_sb = sb("b1_sb", [P, N1])
        b2_sb = sb("b2_sb", [P, N2])
        ident = sb("ident", [P, P])

        block_ps = [ps(f"block_ps{k}", [P, BLOCK, P]) for k in range(2)]
        gram_ps = [ps(f"gram_ps{k}", [P, ROUND, P]) for k in range(2)]
        back_ps = ps("back_ps", [P, PAIR_CHUNKS + 1, P])
        y_ps = back_ps[:, PAIR_CHUNKS, 0:1]
        mlp_ps = ps("mlp_ps", [P, N1, P])
        last_back_ps = [back_ps[:, 0, :], block_ps[0][:, 0, :], block_ps[1][:, 0, :]]
        last_h1_ps = [gram_ps[n // 2][:, (n % 2) * BLOCK, :] for n in range(N1)]
        last_h2_ps = [mlp_ps[:, 0, :], block_ps[1][:, 1, :]]
        last_y_ps = block_ps[0][:, 1, 0:1]
        look_ps = [gram_ps[0][:, 4 * v:4 * v + 4, :].rearrange("d t p -> d (t p)") for v in range(BUFS)]

        row_of_set, gram_blank = sem("row_of_set"), sem("gram_blank")
        table_in = [sem(f"table_in{v}") for v in range(BUFS)]
        half_table_in = sem("half_table_in")
        first_ids_in, second_ids_in, hot_ids_in = sem("first_ids_in"), sem("second_ids_in"), sem("hot_ids_in")
        measuring, measured = sem("measuring"), sem("measured")
        hi_ready, lo_ready = sem("hi_ready"), sem("lo_ready")
        half_hi_ready, half_lo_ready = sem("half_hi_ready"), sem("half_lo_ready")
        dve_onehots, act_onehots = sem("dve_onehots"), sem("act_onehots")
        looked_up = sem("looked_up")
        comparing, emptying, looked_ready = sem("comparing"), sem("emptying"), sem("looked_ready")
        last_look_emptied = sem("last_look_emptied")
        ids_in, dense_in = sem("ids_in"), sem("dense_in")
        rows_in = [[sem(f"rows_in{t}_{q}") for q in range(BLOCKS)] for t in range(TILES)]
        weights_in, biases_in = sem("weights_in"), sem("biases_in")
        ident_blank, ident_set, pads_set = sem("ident_blank"), sem("ident_set"), sem("pads_set")
        blocks_up = sem("blocks_up")
        dve_blocks, act_blocks = sem("dve_blocks"), sem("act_blocks")
        rounds_up = sem("rounds_up")
        dve_rounds, act_rounds = sem("dve_rounds"), sem("act_rounds")
        turned_ready, packed = sem("turned_ready"), sem("packed")
        back_up, pairs_ready = sem("back_up"), sem("pairs_ready")
        h1_up, h1_ready = sem("h1_up"), sem("h1_ready")
        h2_up, h2_ready = sem("h2_up"), sem("h2_ready")
        y_up, y_ready = sem("y_up"), sem("y_ready")
        last_packed = [sem(f"last_packed{c}") for c in range(PAIR_CHUNKS)]
        last_back_up = sem("last_back_up")
        last_pairs_ready = [sem(f"last_pairs_ready{c}") for c in range(PAIR_CHUNKS)]
        last_h1_up, last_h1_ready = sem("last_h1_up"), sem("last_h1_ready")
        last_h2_up = sem("last_h2_up")
        last_h2_ready = [sem(f"last_h2_ready{m}") for m in range(N2)]
        stored = sem("stored")

        DB, AB = (BLOCKS + 1) // 2, BLOCKS // 2
        DVE_DIAGONAL, ACT_DIAGONAL = range(GROUP // 2), range(GROUP // 2, GROUP)

        def places(q):
            return range(BLOCK * q, min(BLOCK * (q + 1), COLD + 1))

        def spread(q, t):
            n = len(places(q))
            return (feats_t[:, t, :, :, HOT + BLOCK * q:HOT + BLOCK * q + n].rearrange("d g s f -> d s g f"),
                    block_ps[q % 2][:, 0:n, :].rearrange("d f (s g) -> d s g f", g=SUB))

        def diagonal(r, s):
            rows = slice(SUB * s, SUB * s + FEATS)
            return (gram[rows, :, ROUND * r:ROUND * (r + 1)].rearrange("f j g -> f g j"),
                    gram_ps[r % 2][rows, :, FEATS * s:FEATS * (s + 1)])

        def pairs_of(first, last):
            f, n = CHUNK_F * first, CHUNK_F * (last - first)
            whole = turned[:, :, :]
            return (pairs[:, f:f + n, :],
                    bass.AP(whole.tensor, whole.offset + SUB + (SUB + 1) * f,
                            [list(whole.ap[0]), [SUB + 1, n], [SUB, REACH]]))

        block = ctx.enter_context(nc.Block())

        @block.sync
        def _(sp):
            def load_table(j):
                sp.dma_start(table[j % BUFS][:, :, :], hot_tables[j]).then_inc(table_in[j % BUFS], 16)

            def load_hot_ids(js, signal):
                n = len(js)
                sp.dma_start(hot_ids_all[:, js[0]:js[0] + n, :].rearrange("p j b -> p (j b)"),
                             hot_ids[js[0]:js[0] + n, :].rearrange("j b -> (j b)").unsqueeze(0)
                             .to_broadcast((HOT_P, n * BATCH))).then_inc(signal, 16)

            load_hot_ids(range(0, 1), first_ids_in)
            sp.dma_start(table[0][:, 0:HALF, :], hot_tables[0][:, 0:HALF, :]).then_inc(half_table_in, 16)
            sp.dma_start(table[0][:, HALF:LOOKS, :], hot_tables[0][:, HALF:LOOKS, :]).then_inc(table_in[0], 16)
            load_hot_ids(range(1, 2), second_ids_in)
            load_table(1)
            load_hot_ids(range(2, HOT), hot_ids_in)
            for j in range(BUFS, HOT):
                sp.wait_ge(lo_ready, j - BUFS + 1)
                load_table(j)
            sp.dma_start(emb[:, :, COLD, :], dense).then_inc(dense_in, 16)
            for dst, src in ((b1_sb, b1), (b2_sb, b2)):
                sp.dma_start(dst[:], src).then_inc(biases_in, 16)
            for dst, src in ((w1_sb, w1), (w2_sb, w2), (w3_sb, w3)):
                sp.dma_start(dst[:], src).then_inc(weights_in, 16)
            sp.wait_ge(y_ready, TILES)
            sp.dma_start(out.rearrange("(p t) n -> p (t n)", t=TILES), y_all[:, :]).then_inc(stored, 16)
            sp.wait_ge(stored, 16)

        @block.gpsimd
        def _(pool):
            nc.gpsimd.iota(row_of[:, :], [[1, LOOKS]], base=0, channel_multiplier=LOOKS,
                           allow_small_or_imprecise_dtypes=True).then_inc(row_of_set, 1)
            pool.wait_ge(ident_blank, 1)
            nc.gpsimd.affine_select(out=ident[:, :], in_=ident[:, :], compare_op=ALU.not_equal, fill=1.0,
                                    base=0, pattern=[[-1, P]], channel_multiplier=1).then_inc(ident_set, 1)
            pool.wait_ge(ids_in, 16)
            for t in range(TILES):
                for n in range(COLD):
                    nc.gpsimd.indirect_dma_start(
                        emb[:, t, n, :], None, tables[n],
                        bass.IndirectOffsetOnAxis(ap=ids_all[:, t, n:n + 1], axis=0),
                    ).then_inc(rows_in[t][n // BLOCK], 16)

        @block.vector
        def _(dve):
            nc.vector.memset(ident[:, :], 0.0).then_inc(ident_blank, 1)
            nc.vector.memset(gram[:, :, :], 0.0).then_inc(gram_blank, 1)

            def pads(tiles):
                nc.vector.memset(feats_t[:, tiles, :, :, FEATS:SUB], 0.0).then_inc(pads_set, 1)

            pads(slice(0, TILES // 2))
            dve.wait_ge(row_of_set, 1)

            FIRST, REST = range(DVE_LOOKS // 2), range(DVE_LOOKS // 2, DVE_LOOKS)

            def onehots(v, n, cs):
                j = BUFS * n + v
                dve.wait_ge(looked_up, j + 1)
                dve.sem_inc(comparing, 1)
                for c in cs:
                    nc.vector.tensor_scalar(onehot[v][:, c:c + 1, :], hot_ids_all[:, bass.ds(j, 1), :],
                                            row_of[:, c:c + 1], None, ALU.is_equal).then_inc(dve_onehots, 1)

            def low_part(v, n):
                dve.wait_ge(looked_up, BUFS * n + v + 1)
                dve.wait_ge(hi_ready, BUFS * n + v + 1)
                nc.vector.tensor_tensor(table_lo[v][:, :, :], table[v][:, :, :],
                                        table_hi[v][:, :, :].bitcast(f32), ALU.subtract).then_inc(lo_ready, 1)

            dve.wait_ge(first_ids_in, 16)
            onehots(0, 0, range(DVE_LOOKS))
            for cs, high, low in ((slice(0, HALF), half_hi_ready, half_lo_ready),
                                  (slice(HALF, LOOKS), hi_ready, lo_ready)):
                dve.wait_ge(high, 1)
                nc.vector.tensor_tensor(table_lo[0][:, cs, :], table[0][:, cs, :],
                                        table_hi[0][:, cs, :].bitcast(f32), ALU.subtract).then_inc(low, 1)
            dve.wait_ge(second_ids_in, 16)
            onehots(1, 0, FIRST)
            low_part(1, 0)
            onehots(1, 0, REST)
            dve.wait_ge(hot_ids_in, 16)
            with dve.Fori(1, HOT // BUFS) as i:
                for v in range(BUFS):
                    onehots(v, i, FIRST)
                    low_part(v, i)
                    onehots(v, i, REST)
            pads(slice(TILES // 2, TILES))

            def blocks(t, qs):
                for q in qs:
                    dve.wait_ge(blocks_up, BLOCKS * t + q + 1)
                    dst, src = spread(q, t)
                    last = nc.vector.tensor_copy(dst, src)
                    if COLD in places(q):
                        last = nc.vector.tensor_copy(dense_t[:, t % 2, :], block_ps[q % 2][:, COLD % BLOCK, :])
                    last.then_inc(dve_blocks, 1)

            def gram_round(t, r):
                dve.wait_ge(rounds_up, ROUNDS * t + r + 1)
                for s in DVE_DIAGONAL:
                    dst, src = diagonal(r, s)
                    last = nc.vector.tensor_copy(dst, src)
                last.then_inc(dve_rounds, 1)

            def turn_first(t):
                dve.wait_ge(act_rounds, ROUNDS * (t + 1))
                dve.wait_ge(dve_rounds, ROUNDS * (t + 1))
                nc.vector.transpose(turned[:, 1:TURN, :], gram[:, 1:TURN, :]).then_inc(turned_ready, 1)

            def turn_rest(t):
                nc.vector.transpose(turned[:, TURN:FEATS, :], gram[:, TURN:FEATS, :])
                nc.vector.transpose(turned[:, FEATS:WIDE, :], gram[:, 0:REACH, :]).then_inc(turned_ready, 1)

            def layer2(t):
                dve.wait_ge(h2_up, t + 1)
                for m in range(N2):
                    last = nc.vector.tensor_scalar(h2[:, m, :], mlp_ps[:, m, :], b2_sb[:, m:m + 1], 0.0,
                                                   ALU.add, ALU.max)
                last.then_inc(h2_ready, 1)

            def layer3(t):
                dve.wait_ge(y_up, t + 1)
                nc.vector.tensor_copy(y_all[:, t:t + 1], y_ps).then_inc(y_ready, 1)

            dve.wait_ge(biases_in, 16 * 2)
            dve.wait_ge(gram_blank, 1)
            blocks(0, range(0, BLOCKS, 2))
            for t in range(TILES):
                for r in range(ROUNDS):
                    gram_round(t, r)
                if t == 0:
                    blocks(1, [0])
                turn_first(t)
                if 0 < t < TILES - 1:
                    layer2(t - 1)
                turn_rest(t)
                if 0 < t < TILES - 1:
                    blocks(t + 1, [0])
                    layer3(t - 1)
                if t + 1 < TILES:
                    blocks(t + 1, range(2, BLOCKS, 2))

            dve.wait_ge(turned_ready, 2 * TILES)
            dst, src = pairs_of(1, 2)
            nc.vector.tensor_copy(dst, src).then_inc(last_packed[1], 1)
            layer2(TILES - 2)
            dve.wait_ge(last_back_up, 2)
            nc.vector.tensor_copy(pairs_t[0:CHUNK, 1, :], last_back_ps[1][0:CHUNK, :]).then_inc(last_pairs_ready[1], 1)
            layer3(TILES - 2)
            dve.wait_ge(last_h2_up, 1)
            nc.vector.tensor_scalar(h2[:, 0, :], last_h2_ps[0], b2_sb[:, 0:1], 0.0,
                                    ALU.add, ALU.max).then_inc(last_h2_ready[0], 1)
            dve.wait_ge(y_up, TILES)
            nc.vector.tensor_copy(y_all[:, TILES - 1:TILES], last_y_ps).then_inc(y_ready, 1)

        @block.scalar
        def _(act):
            act.sem_inc(looked_ready, BUFS)

            def high_part(v, n):
                act.wait_ge(table_in[v], 16 * (n + 1))
                act.wait_ge(looked_up, BUFS * n + v + 1)
                nc.scalar.copy(table_hi[v][:, :, :], table[v][:, :, :]).then_inc(hi_ready, 1)

            def measure(v, n):
                j = BUFS * n + v
                act.wait_ge(looked_up, j + 1)
                act.sem_inc(measuring, 1)
                for c in range(DVE_LOOKS, LOOKS):
                    last = nc.scalar.activation(onehot[v][:, c:c + 1, :], hot_ids_all[:, bass.ds(j, 1), :], ACT.Abs,
                                                bias=row_of[:, c:c + 1], scale=-1.0)
                last.then_inc(measured, 1)

            def onehots(v, n):
                act.wait_ge(measured, BUFS * n + v + 1)
                nc.scalar.activation(onehot[v][:, DVE_LOOKS:LOOKS, :],
                                     onehot[v][:, DVE_LOOKS:LOOKS, :].bitcast(f32), ACT.Relu,
                                     bias=1.0, scale=-1.0).then_inc(act_onehots, 1)

            def place(v, j, tiles):
                dst = feats_t[:, tiles, :, :, bass.ds(j, 1)].rearrange("d t g s f -> d (t f) s g")
                src = look_ps[v].rearrange("d (t s g) -> d t s g", t=TILES, s=GROUP)[:, tiles]
                return nc.scalar.copy(dst, src)

            def empty(v, n):
                j = BUFS * n + v
                act.wait_ge(looked_up, BUFS + j + 1)
                act.sem_inc(emptying, 1)
                place(v, j, slice(0, TILES)).then_inc(looked_ready, 1)

            act.dma_start(ids_all[:, :, :], ids).then_inc(ids_in, 16)
            nc.scalar.preload_act_table(ACT.Relu)
            act.wait_ge(row_of_set, 1)
            act.wait_ge(first_ids_in, 16)
            measure(0, 0)
            act.wait_ge(half_table_in, 16)
            nc.scalar.copy(table_hi[0][:, 0:HALF, :], table[0][:, 0:HALF, :]).then_inc(half_hi_ready, 1)
            act.wait_ge(table_in[0], 16)
            nc.scalar.copy(table_hi[0][:, HALF:LOOKS, :], table[0][:, HALF:LOOKS, :]).then_inc(hi_ready, 1)
            onehots(0, 0)
            act.wait_ge(second_ids_in, 16)
            high_part(1, 0)
            measure(1, 0)
            onehots(1, 0)
            act.wait_ge(hot_ids_in, 16)
            with act.Fori(1, HOT // BUFS) as i:
                for v in range(BUFS):
                    high_part(v, i)
                    empty(v, i - 1)
                    measure(v, i)
                    onehots(v, i)
            empty(0, HOT // BUFS - 1)

            def blocks(t, qs):
                for q in qs:
                    act.wait_ge(blocks_up, BLOCKS * t + q + 1)
                    dst, src = spread(q, t)
                    nc.scalar.copy(dst, src).then_inc(act_blocks, 1)

            def gram_round(t, r):
                act.wait_ge(rounds_up, ROUNDS * t + r + 1)
                if r == 0 and t > 0:
                    act.wait_ge(turned_ready, 2 * t)
                for s in ACT_DIAGONAL:
                    dst, src = diagonal(r, s)
                    last = nc.scalar.copy(dst, src)
                last.then_inc(act_rounds, 1)

            def pack(t):
                act.wait_ge(turned_ready, 2 * (t + 1))
                nc.scalar.copy(*pairs_of(0, PAIR_CHUNKS)).then_inc(packed, 1)

            def back(t):
                act.wait_ge(back_up, t + 1)
                nc.scalar.copy(pairs_t[0:CHUNK, :, :], back_ps[0:CHUNK, 0:PAIR_CHUNKS, :]
                               ).then_inc(pairs_ready, 1)

            def layer1(t):
                act.wait_ge(h1_up, t + 1)
                for n in range(N1):
                    last = nc.scalar.activation(h1[:, n, :], mlp_ps[:, n, :], ACT.Relu, bias=b1_sb[:, n:n + 1])
                last.then_inc(h1_ready, 1)

            act.wait_ge(biases_in, 16 * 2)
            act.wait_ge(gram_blank, 1)
            blocks(0, range(1, BLOCKS, 2))
            act.wait_ge(looked_up, BUFS + HOT)
            place(1, HOT - 1, slice(0, 1)).then_inc(looked_ready, 1)
            place(1, HOT - 1, slice(1, TILES)).then_inc(last_look_emptied, 1)
            for t in range(TILES):
                gram_round(t, 0)
                if t > 0:
                    layer1(t - 1)
                for r in range(1, ROUNDS):
                    gram_round(t, r)
                if t + 1 < TILES:
                    blocks(t + 1, [1])
                if t + 1 < TILES:
                    pack(t)
                    back(t)
                    blocks(t + 1, range(3, BLOCKS, 2))

            act.wait_ge(turned_ready, 2 * TILES - 1)
            nc.scalar.copy(*pairs_of(0, 1)).then_inc(last_packed[0], 1)
            act.wait_ge(turned_ready, 2 * TILES)
            nc.scalar.copy(*pairs_of(2, 3)).then_inc(last_packed[2], 1)
            for c in (0, 2):
                act.wait_ge(last_back_up, c + 1)
                nc.scalar.copy(pairs_t[0:CHUNK, c, :], last_back_ps[c][0:CHUNK, :]).then_inc(last_pairs_ready[c], 1)
            for n in range(N1):
                act.wait_ge(last_h1_up, n + 1)
                nc.scalar.activation(h1[:, n, :], last_h1_ps[n], ACT.Relu,
                                     bias=b1_sb[:, n:n + 1]).then_inc(last_h1_ready, 1)
            act.wait_ge(last_h2_up, 2)
            nc.scalar.activation(h2[:, 1, :], last_h2_ps[1], ACT.Relu, bias=b2_sb[:, 1:2]).then_inc(last_h2_ready[1], 1)

        @block.tensor
        def _(pe):
            def look_high(v, n, cs, first=False):
                j = BUFS * n + v
                for c in cs:
                    if c == 0:
                        pe.wait_ge(looked_ready, j + 1)
                    if c == 0 and first:
                        pe.wait_ge(half_hi_ready, 1)
                    if c == (HALF if first else 0):
                        pe.wait_ge(hi_ready, j + 1)
                    if c < DVE_LOOKS:
                        pe.wait_ge(dve_onehots, DVE_LOOKS * j + c + 1)
                    elif c == DVE_LOOKS:
                        pe.wait_ge(act_onehots, j + 1)
                    nc.tensor.matmul(look_ps[v], table_hi[v][:, c, :], onehot[v][:, c, :],
                                     start=(c == 0), stop=False)

            def look_low(v, n, cs, first=False):
                for c in cs:
                    if c == 0 and first:
                        pe.wait_ge(half_lo_ready, 1)
                    if c == (HALF if first else 0):
                        pe.wait_ge(lo_ready, BUFS * n + v + 1)
                    last = nc.tensor.matmul(look_ps[v], table_lo[v][:, c, :], onehot[v][:, c, :],
                                            start=False, stop=(c == LOOKS - 1))
                if LOOKS - 1 in cs:
                    last.then_inc(looked_up, 1)

            FIRST, REST = range(DVE_LOOKS), range(DVE_LOOKS, LOOKS)

            def look_up(v, n, first=False):
                look_high(v, n, FIRST, first)
                look_low(v, n, FIRST, first)
                look_high(v, n, REST, first)
                look_low(v, n, REST, first)

            def blocks(t, qs):
                for q in qs:
                    pe.wait_ge(rows_in[t][q], 16 * sum(n < COLD for n in places(q)))
                    if q % 2 == 0 and DB * t + q // 2 > 0:
                        pe.wait_ge(dve_blocks, DB * t + q // 2)
                    if q % 2 == 1 and AB * t + q // 2 > 0:
                        pe.wait_ge(act_blocks, AB * t + q // 2)
                    for n in places(q):
                        last = nc.tensor.transpose(block_ps[q % 2][:, n % BLOCK, :], emb[:, t, n, :], ident[:, :])
                    last.then_inc(blocks_up, 1)

            def gram_rounds(t):
                pe.wait_ge(dve_blocks, DB * (t + 1))
                pe.wait_ge(act_blocks, AB * (t + 1))
                for r in range(ROUNDS):
                    before = ROUNDS * t + r - 2
                    if t == 0 and r == 0:
                        pe.wait_ge(looked_ready, BUFS + HOT)
                    elif before >= 0:
                        pe.wait_ge(dve_rounds, before + 1)
                        pe.wait_ge(act_rounds, before + 1)
                    for k in range(ROUND):
                        g = ROUND * r + k
                        if t == 0 and r == 0 and k == BLOCK:
                            pe.wait_ge(last_look_emptied, 1)
                        four = feats_t[:, t, g, :, :].rearrange("d s f -> d (s f)")[:, 0:GRAM_ROWS]
                        last = nc.tensor.matmul(gram_ps[r % 2][0:GRAM_ROWS, k, 0:GROUP * FEATS], four,
                                                feats_t[:, t, g, :, 0:FEATS], start=True, stop=True)
                    last.then_inc(rounds_up, 1)

            def back(t):
                if t > 0:
                    pe.wait_ge(pairs_ready, t)
                    pe.wait_ge(y_ready, t)
                pe.wait_ge(packed, t + 1)
                for c in range(PAIR_CHUNKS):
                    last = nc.tensor.transpose(back_ps[0:CHUNK, c, :], pairs[:, CHUNK_F * c:CHUNK_F * (c + 1), :],
                                               ident[:, :])
                last.then_inc(back_up, 1)

            def layer1_dense(t):
                if t > 0:
                    pe.wait_ge(h2_ready, t)
                for n in range(N1):
                    nc.tensor.matmul(mlp_ps[:, n, :], w1_sb[:, PAIR_CHUNKS, P * n:P * (n + 1)], dense_t[:, t % 2, :],
                                     start=(n == 0), stop=False, skip_group_check=True)

            def layer1_pairs(t, ns):
                pe.wait_ge(pairs_ready, t + 1)
                for n in ns:
                    for c in range(PAIR_CHUNKS):
                        last = nc.tensor.matmul(mlp_ps[:, n, :], w1_sb[0:CHUNK, c, P * n:P * (n + 1)],
                                                pairs_t[0:CHUNK, c, :], start=False, stop=(c == PAIR_CHUNKS - 1),
                                                skip_group_check=True)
                if N1 - 1 in ns:
                    last.then_inc(h1_up, 1)

            def layer2(t):
                pe.wait_ge(h1_ready, t + 1)
                for m in range(N2):
                    for n in range(N1):
                        last = nc.tensor.matmul(mlp_ps[:, m, :], w2_sb[:, n, P * m:P * (m + 1)], h1[:, n, :],
                                                start=(n == 0), stop=(n == N1 - 1))
                last.then_inc(h2_up, 1)

            def layer3(t):
                pe.wait_ge(h2_ready, t + 1)
                for m in range(N2):
                    last = nc.tensor.matmul(y_ps, h2[:, m, :], w3_sb[:, m:m + 1],
                                            start=(m == 0), stop=(m == N2 - 1))
                last.then_inc(y_up, 1)

            pe.sem_inc(looked_up, BUFS)
            pe.wait_ge(ident_set, 1)
            for k in range(WARM):
                nc.tensor.transpose(back_ps[:, k % PAIR_CHUNKS, :], ident[:, :], ident[:, :])
            look_up(0, 0, first=True)
            look_up(1, 0)
            with pe.Fori(1, HOT // BUFS - 1) as i:
                for v in range(BUFS):
                    look_up(v, i)
            pe.wait_ge(dense_in, 16)
            look_up(0, HOT // BUFS - 1)
            blocks(0, [0, 1])
            look_high(1, HOT // BUFS - 1, FIRST)
            look_low(1, HOT // BUFS - 1, FIRST)
            blocks(0, [2, 3])
            look_high(1, HOT // BUFS - 1, REST)
            blocks(0, range(4, BLOCKS))
            look_low(1, HOT // BUFS - 1, REST)
            pe.wait_ge(pads_set, 2)
            for t in range(TILES - 1):
                gram_rounds(t)
                if t > 0:
                    layer2(t - 1)
                blocks(t + 1, [0, 1])
                if t > 0:
                    layer3(t - 1)
                else:
                    pe.wait_ge(weights_in, 16 * 3)
                layer1_dense(t)
                if t > 0:
                    back(t)
                    blocks(t + 1, [2, 3])
                else:
                    blocks(t + 1, [2, 3])
                    back(t)
                layer1_pairs(t, range(0, 1))
                blocks(t + 1, range(4, BLOCKS))
                layer1_pairs(t, range(1, N1))

            gram_rounds(TILES - 1)
            layer2(TILES - 2)

            def last_back(c):
                pe.wait_ge(last_packed[c], 1)
                nc.tensor.transpose(last_back_ps[c][0:CHUNK, :], pairs[:, CHUNK_F * c:CHUNK_F * (c + 1), :],
                                    ident[:, :]).then_inc(last_back_up, 1)

            def last_dense(ns):
                for n in ns:
                    nc.tensor.matmul(last_h1_ps[n], w1_sb[:, PAIR_CHUNKS, P * n:P * (n + 1)],
                                     dense_t[:, (TILES - 1) % 2, :], start=True, stop=False)

            pe.wait_ge(dve_rounds, ROUNDS * TILES - 1)
            pe.wait_ge(act_rounds, ROUNDS * TILES - 1)
            last_dense(range(0, N1 // 2))
            last_back(0)
            pe.wait_ge(dve_rounds, ROUNDS * TILES)
            pe.wait_ge(act_rounds, ROUNDS * TILES)
            last_dense(range(N1 // 2, N1))
            for c in range(1, PAIR_CHUNKS):
                last_back(c)

            def pairs_products(n, c):
                last = nc.tensor.matmul(last_h1_ps[n], w1_sb[0:CHUNK, c, P * n:P * (n + 1)], pairs_t[0:CHUNK, c, :],
                                        start=False, stop=(c == PAIR_CHUNKS - 1))
                if c == PAIR_CHUNKS - 1:
                    last.then_inc(last_h1_up, 1)

            pe.wait_ge(last_pairs_ready[0], 1)
            for n in range(N1):
                pairs_products(n, 0)
            for c in range(1, PAIR_CHUNKS):
                pe.wait_ge(last_pairs_ready[c], 1)
            layer3(TILES - 2)
            for n in range(N1 + 2):
                if n < N1:
                    for c in range(1, PAIR_CHUNKS):
                        pairs_products(n, c)
                if n >= 2:
                    pe.wait_ge(last_h1_ready, n - 1)
                    for m in range(N2):
                        last = nc.tensor.matmul(last_h2_ps[m], w2_sb[:, n - 2, P * m:P * (m + 1)], h1[:, n - 2, :],
                                                start=(n == 2), stop=(n == N1 + 1))
                        if n == N1 + 1:
                            last.then_inc(last_h2_up, 1)
            for m in range(N2):
                pe.wait_ge(last_h2_ready[m], 1)
                last = nc.tensor.matmul(last_y_ps, h2[:, m, :], w3_sb[:, m:m + 1], start=(m == 0), stop=(m == N2 - 1))
            last.then_inc(y_up, 1)


def kernel(**inputs):
    import numpy as np
    import concourse.bacc as bacc
    from concourse.bass_utils import run_bass_kernel_spmd

    at = {}
    for i in range(FEATS):
        for j in range(i + 1, FEATS):
            at[i, j] = len(at)
    w_top1 = np.asarray(inputs["W_top1"])
    w1 = np.zeros((K1, P, HID1), w_top1.dtype)
    for f in range(FEATS):
        for delta in range(1, REACH + 1):
            i, j = sorted((ORDER[f], ORDER[(f + delta) % FEATS]))
            w1[f // CHUNK_F, (f % CHUNK_F) * REACH + delta - 1] = w_top1[at[i, j]]
    w1[PAIR_CHUNKS] = w_top1[len(at):]

    def chunks(a, n):
        return np.ascontiguousarray(np.asarray(a).reshape(n, P, -1).transpose(1, 0, 2))

    ids = np.asarray(inputs["ids"]).reshape(P, TILES, TABLES)
    arrays = {
        "ids": np.ascontiguousarray(ids[:, :, COLD_TABLES]),
        "hot_ids": np.ascontiguousarray(ids[:, :, HOT_TABLES].transpose(2, 1, 0)).reshape(HOT, BATCH),
        "dense": np.ascontiguousarray(inputs["r_dense_x"]).reshape(P, TILES, DIM),
        "w1": np.ascontiguousarray(w1.transpose(1, 0, 2)),
        "b1": chunks(inputs["b_top1"], N1).reshape(P, N1),
        "w2": chunks(inputs["W_top2"], N1),
        "b2": chunks(inputs["b_top2"], N2).reshape(P, N2),
        "w3": chunks(inputs["W_top3"], N2).reshape(P, N2),
    }
    for f in range(TABLES):
        shape = (HOT_P, LOOKS, DIM) if f in HOT_TABLES else (ROWS[f], DIM)
        arrays[f"tbl_{f}"] = np.ascontiguousarray(inputs[f"tbl_{f}"]).reshape(shape)

    nc = bacc.Bacc("TRN2", target_bir_lowering=False, num_devices=1)
    ap = {name: nc.dram_tensor(name, a.shape, mybir.dt.from_np(a.dtype), kind="ExternalInput").ap()
          for name, a in arrays.items()}
    out = nc.dram_tensor("out", (BATCH, 1), mybir.dt.float32, kind="ExternalOutput").ap()
    tower(nc, ap["ids"], ap["hot_ids"], ap["dense"], [ap[f"tbl_{f}"] for f in HOT_TABLES],
          [ap[f"tbl_{f}"] for f in COLD_TABLES], ap["w1"], ap["b1"], ap["w2"], ap["b2"], ap["w3"], out)
    return run_bass_kernel_spmd(nc, [arrays], core_ids=[0]).results[0]["out"]
```
